# Optimizing a Trainium2 kernel written in Bass

```python
import numpy as np
import jax
import jax.numpy as jnp

def _softmax(x, axis=-1):
    return jax.nn.softmax(x, axis=axis)

def _gelu(x):
    return jax.nn.gelu(x, approximate=True)

def _silu(x):
    return jax.nn.silu(x)

def _sigmoid(x):
    return jax.nn.sigmoid(x)

def _layernorm(x, axis=-1, eps=1e-05):
    m = jnp.mean(x, axis=axis, keepdims=True)
    v = jnp.var(x, axis=axis, keepdims=True)
    return (x - m) / jnp.sqrt(v + eps)

def _scatter_add(tgt, idx, src, axis=0):
    return tgt.at[idx].add(src)

def _segment_sum(src, seg, n):
    return jax.ops.segment_sum(src, seg, n)
kernel_name = 'mk_decoder_postln_d1_seqx_r8_b2415b'

def setup_inputs(seed: int=0):
    np.random.seed(seed)
    _w = jnp.asarray

    def _rec_inputs():
        import jax
        import jax.numpy as jnp
        _rk = jax.random.key(seed)
        x = 7.22e-05 + 1 * jax.random.normal(jax.random.fold_in(_rk, 1), (8, 128, 512), jnp.float32)
        _lenS = 128 - jax.random.randint(jax.random.fold_in(_rk, 7), (8,), 0, max(1, 128 // 4) + 1, jnp.int32)
        _lenS2 = 128 - jax.random.randint(jax.random.fold_in(_rk, 8), (8,), 0, max(1, 128 // 4) + 1, jnp.int32)
        _ctx_4096P = jax.random.normal(jax.random.fold_in(_rk, 11), (8, 16, 512), jnp.float32)
        _ctx_4096c = jax.random.dirichlet(jax.random.fold_in(_rk, 511), 0.3 * jnp.ones((16,), jnp.float32), (8, 128))
        _ctx_4096t = jnp.einsum('bsk,bkd->bsd', _ctx_4096c, _ctx_4096P)
        _ctx_4096t = _ctx_4096t * jax.lax.rsqrt(jnp.mean(jnp.square(_ctx_4096t)) + 1e-12) * 0.953939
        ctx_4096 = 4.13588e-05 + 0.999923 * (_ctx_4096t + 0.3 * jax.random.normal(jax.random.fold_in(_rk, 611), (8, 128, 512), jnp.float32))
        _validS = jnp.arange(128)[None, :] < _lenS[:, None]
        _validS2 = jnp.arange(128)[None, :] < _lenS2[:, None]
        _causal = jnp.tril(jnp.ones((128, 128), dtype=bool))
        mask_BxSxS2_ff1 = jnp.where(jnp.ones((8, 128, 128), dtype=bool), 1.0, 0.0).astype(jnp.float32)
        return (x, ctx_4096, mask_BxSxS2_ff1)
    x, ctx_4096, mask_BxSxS2_ff1 = _rec_inputs()

    def _L0_attn_setup():
        import jax, jax.numpy as jnp
        import numpy as np
        import math
        B, L, D, H = (32, 64, 512, 32)
        HD = D // H
        key = jax.random.key(seed)
        ks = jax.random.split(key, 9)
        s = 1.0 / math.sqrt(D)
        return {'x': jax.random.normal(ks[0], (B, L, D), jnp.float32), 'Wq': jax.random.normal(ks[1], (D, D), jnp.float32) * s, 'bq': jax.random.normal(ks[2], (D,), jnp.float32) * s, 'Wk': jax.random.normal(ks[3], (D, D), jnp.float32) * s, 'bk': jax.random.normal(ks[4], (D,), jnp.float32) * s, 'Wv': jax.random.normal(ks[5], (D, D), jnp.float32) * s, 'bv': jax.random.normal(ks[6], (D,), jnp.float32) * s, 'Wo': jax.random.normal(ks[7], (D, D), jnp.float32) * s, 'bo': jax.random.normal(ks[8], (D,), jnp.float32) * s}
    _L0_attn_all = _L0_attn_setup()
    _L0_attn_in = {k: v for k, v in _L0_attn_all.items() if k in ('Wq', 'bq', 'Wk', 'bk', 'Wv', 'bv', 'Wo', 'bo')}
    del _L0_attn_all

    def _L0_xattn_setup():
        import jax, jax.numpy as jnp
        import numpy as np
        N_Q_HEADS = 32
        N_KV_HEADS = 8
        D_MODEL = 512
        D_K = 128
        D_V = 128
        ROPE_BASE = 10000.0

        def _rope(x):
            d = x.shape[-1]
            s = x.shape[2]
            inv_freq = 1.0 / ROPE_BASE ** (jnp.arange(0, d, 2, dtype=jnp.float32) / d)
            ang = jnp.arange(s, dtype=jnp.float32)[:, None] * inv_freq[None, :]
            cos = jnp.concatenate([jnp.cos(ang), jnp.cos(ang)], axis=-1)[None, None]
            sin = jnp.concatenate([jnp.sin(ang), jnp.sin(ang)], axis=-1)[None, None]
            x1, x2 = (x[..., :d // 2], x[..., d // 2:])
            rot = jnp.concatenate([-x2, x1], axis=-1)
            return x * cos + rot * sin
        key = jax.random.key(seed)
        ks = jax.random.split(key, 8)
        bs, s = (2, 128)
        inp = {'query': jax.random.normal(ks[0], (bs, s, D_MODEL), dtype=jnp.float32), 'key': jax.random.normal(ks[1], (bs, s, D_MODEL), dtype=jnp.float32), 'value': jax.random.normal(ks[2], (bs, s, D_MODEL), dtype=jnp.float32), 'mask': jnp.ones((bs, s, s), dtype=jnp.float32), 'wq': jax.random.normal(ks[3], (D_MODEL, N_Q_HEADS * D_K), dtype=jnp.float32) * 0.02, 'wk': jax.random.normal(ks[4], (D_MODEL, N_KV_HEADS * D_K), dtype=jnp.float32) * 0.02, 'wv': jax.random.normal(ks[5], (D_MODEL, N_KV_HEADS * D_V), dtype=jnp.float32) * 0.02, 'wo': jax.random.normal(ks[6], (N_Q_HEADS * D_V, D_MODEL), dtype=jnp.float32) * 0.02}
        return inp
    _L0_xattn_all = _L0_xattn_setup()
    _L0_xattn_in = {k: v for k, v in _L0_xattn_all.items() if k in ('wq', 'wk', 'wv', 'wo')}
    del _L0_xattn_all

    def _L0_ffn_setup():
        import jax, jax.numpy as jnp
        import numpy as np
        HIDDEN = 512
        INTER = 1376
        GROUPSIZE = 128
        PACK = 8

        def dequant_gptq(qweight, scales, zeros, groupsize):
            K = qweight.shape[0] * PACK
            N = qweight.shape[1]
            k = jnp.arange(K)
            q = qweight[k // PACK, :] >> (k % PACK * 4)[:, None] & 15
            n = jnp.arange(N)
            z = zeros[:, n // PACK] >> (n % PACK * 4)[None, :] & 15
            s = scales.astype(jnp.float32)
            zp = (z.astype(jnp.float32) + 1.0) * s
            g = k // groupsize
            return q.astype(jnp.float32) * s[g] - zp[g]
        key = jax.random.key(seed)
        ks = jax.random.split(key, 11)
        imax = 2147483647
        G_h = HIDDEN // GROUPSIZE
        G_i = (INTER + GROUPSIZE - 1) // GROUPSIZE
        x = (jax.random.normal(ks[0], (2, 256, HIDDEN), dtype=jnp.float32) * 0.5).astype(jnp.float16)
        return {'x': x, 'gate_qweight': jax.random.randint(ks[1], (HIDDEN // PACK, INTER), 0, imax, dtype=jnp.int32), 'gate_scales': (jax.random.uniform(ks[2], (G_h, INTER), dtype=jnp.float32) * 0.01 + 0.001).astype(jnp.float16), 'gate_zeros': jax.random.randint(ks[3], (G_h, INTER // PACK), 0, imax, dtype=jnp.int32), 'up_qweight': jax.random.randint(ks[4], (HIDDEN // PACK, INTER), 0, imax, dtype=jnp.int32), 'up_scales': (jax.random.uniform(ks[5], (G_h, INTER), dtype=jnp.float32) * 0.01 + 0.001).astype(jnp.float16), 'up_zeros': jax.random.randint(ks[6], (G_h, INTER // PACK), 0, imax, dtype=jnp.int32), 'down_qweight': jax.random.randint(ks[7], (INTER // PACK, HIDDEN), 0, imax, dtype=jnp.int32), 'down_scales': (jax.random.uniform(ks[8], (G_i, HIDDEN), dtype=jnp.float32) * 0.01 + 0.001).astype(jnp.float16), 'down_zeros': jax.random.randint(ks[9], (G_i, HIDDEN // PACK), 0, imax, dtype=jnp.int32)}
    _L0_ffn_all = _L0_ffn_setup()
    _L0_ffn_in = {k: v for k, v in _L0_ffn_all.items() if k in ('gate_qweight', 'gate_scales', 'gate_zeros', 'up_qweight', 'up_scales', 'up_zeros', 'down_qweight', 'down_scales', 'down_zeros')}
    del _L0_ffn_all
    return {'x': x, 'ctx_4096': ctx_4096, 'mask_BxSxS2_ff1': mask_BxSxS2_ff1, 'L0_attn_Wq': _L0_attn_in['Wq'], 'L0_attn_bq': _L0_attn_in['bq'], 'L0_attn_Wk': _L0_attn_in['Wk'], 'L0_attn_bk': _L0_attn_in['bk'], 'L0_attn_Wv': _L0_attn_in['Wv'], 'L0_attn_bv': _L0_attn_in['bv'], 'L0_attn_Wo': _L0_attn_in['Wo'], 'L0_attn_bo': _L0_attn_in['bo'], 'L0_xattn_wq': _L0_xattn_in['wq'], 'L0_xattn_wk': _L0_xattn_in['wk'], 'L0_xattn_wv': _L0_xattn_in['wv'], 'L0_xattn_wo': _L0_xattn_in['wo'], 'L0_ffn_gate_qweight': _L0_ffn_in['gate_qweight'], 'L0_ffn_gate_scales': _L0_ffn_in['gate_scales'], 'L0_ffn_gate_zeros': _L0_ffn_in['gate_zeros'], 'L0_ffn_up_qweight': _L0_ffn_in['up_qweight'], 'L0_ffn_up_scales': _L0_ffn_in['up_scales'], 'L0_ffn_up_zeros': _L0_ffn_in['up_zeros'], 'L0_ffn_down_qweight': _L0_ffn_in['down_qweight'], 'L0_ffn_down_scales': _L0_ffn_in['down_scales'], 'L0_ffn_down_zeros': _L0_ffn_in['down_zeros']}

def reference(x, ctx_4096, mask_BxSxS2_ff1, L0_attn_Wq, L0_attn_bq, L0_attn_Wk, L0_attn_bk, L0_attn_Wv, L0_attn_bv, L0_attn_Wo, L0_attn_bo, L0_xattn_wq, L0_xattn_wk, L0_xattn_wv, L0_xattn_wo, L0_ffn_gate_qweight, L0_ffn_gate_scales, L0_ffn_gate_zeros, L0_ffn_up_qweight, L0_ffn_up_scales, L0_ffn_up_zeros, L0_ffn_down_qweight, L0_ffn_down_scales, L0_ffn_down_zeros):
    import jax
    import jax.numpy as jnp

    def _L0_attn_ref(x, Wq, bq, Wk, bk, Wv, bv, Wo, bo):
        import jax, jax.numpy as jnp
        import numpy as np
        import math
        B, L, D, H = (32, 64, 512, 32)
        HD = D // H
        b, l, d = x.shape
        h, hd = (H, HD)
        q = (x @ Wq.T + bq).reshape(b, l, h, hd).transpose(0, 2, 1, 3)
        k = (x @ Wk.T + bk).reshape(b, l, h, hd).transpose(0, 2, 1, 3)
        v = (x @ Wv.T + bv).reshape(b, l, h, hd).transpose(0, 2, 1, 3)
        scores = jnp.einsum('bhqd,bhkd->bhqk', q, k) / math.sqrt(hd)
        causal = jnp.tril(jnp.ones((l, l), bool))
        scores = jnp.where(causal, scores, -jnp.inf)
        att = jax.nn.softmax(scores, axis=-1)
        out = jnp.einsum('bhqk,bhkd->bhqd', att, v)
        out = out.transpose(0, 2, 1, 3).reshape(b, l, d)
        return out @ Wo.T + bo

    def _L0_xattn_ref(query, key, value, mask, wq, wk, wv, wo):
        import jax, jax.numpy as jnp
        import numpy as np
        N_Q_HEADS = 32
        N_KV_HEADS = 8
        D_MODEL = 512
        D_K = 128
        D_V = 128
        ROPE_BASE = 10000.0

        def _rope(x):
            d = x.shape[-1]
            s = x.shape[2]
            inv_freq = 1.0 / ROPE_BASE ** (jnp.arange(0, d, 2, dtype=jnp.float32) / d)
            ang = jnp.arange(s, dtype=jnp.float32)[:, None] * inv_freq[None, :]
            cos = jnp.concatenate([jnp.cos(ang), jnp.cos(ang)], axis=-1)[None, None]
            sin = jnp.concatenate([jnp.sin(ang), jnp.sin(ang)], axis=-1)[None, None]
            x1, x2 = (x[..., :d // 2], x[..., d // 2:])
            rot = jnp.concatenate([-x2, x1], axis=-1)
            return x * cos + rot * sin
        bs, s, _ = query.shape
        g = N_Q_HEADS // N_KV_HEADS
        q = (query @ wq).reshape(bs, s, N_Q_HEADS, D_K).transpose(0, 2, 1, 3)
        k = (key @ wk).reshape(bs, s, N_KV_HEADS, D_K).transpose(0, 2, 1, 3)
        v = (value @ wv).reshape(bs, s, N_KV_HEADS, D_V).transpose(0, 2, 1, 3)
        q = _rope(q)
        k = _rope(k)
        scale = jnp.sqrt(jnp.float32(D_K))
        qg = q.reshape(bs, N_KV_HEADS, g, s, D_K)
        scores = jnp.einsum('bhgqd,bhkd->bhgqk', qg, k) / scale
        masked = jnp.where(mask[:, None, None].astype(bool), scores, -1000000000.0)
        w = jax.nn.softmax(masked, axis=-1)
        out = jnp.einsum('bhgqk,bhkd->bhgqd', w, v)
        out = out.reshape(bs, N_Q_HEADS, s, D_V).transpose(0, 2, 1, 3).reshape(bs, s, N_Q_HEADS * D_V)
        return out @ wo

    def _L0_ffn_ref(x, gate_qweight, gate_scales, gate_zeros, up_qweight, up_scales, up_zeros, down_qweight, down_scales, down_zeros):
        import jax, jax.numpy as jnp
        import numpy as np
        HIDDEN = 512
        INTER = 1376
        GROUPSIZE = 128
        PACK = 8

        def dequant_gptq(qweight, scales, zeros, groupsize):
            K = qweight.shape[0] * PACK
            N = qweight.shape[1]
            k = jnp.arange(K)
            q = qweight[k // PACK, :] >> (k % PACK * 4)[:, None] & 15
            n = jnp.arange(N)
            z = zeros[:, n // PACK] >> (n % PACK * 4)[None, :] & 15
            s = scales.astype(jnp.float32)
            zp = (z.astype(jnp.float32) + 1.0) * s
            g = k // groupsize
            return q.astype(jnp.float32) * s[g] - zp[g]
        B, S, H = x.shape
        x2 = x.reshape(-1, H).astype(jnp.float32)
        Wg = dequant_gptq(gate_qweight, gate_scales, gate_zeros, GROUPSIZE)
        Wu = dequant_gptq(up_qweight, up_scales, up_zeros, GROUPSIZE)
        Wd = dequant_gptq(down_qweight, down_scales, down_zeros, GROUPSIZE)
        gate = x2 @ Wg
        up = x2 @ Wu
        inter = gate * jax.nn.sigmoid(gate) * up
        out = (inter @ Wd).astype(jnp.float16)
        return out.reshape(B, S, H)
    x = _layernorm(x + _L0_attn_ref(x, L0_attn_Wq, L0_attn_bq, L0_attn_Wk, L0_attn_bk, L0_attn_Wv, L0_attn_bv, L0_attn_Wo, L0_attn_bo), axis=-1)
    x = _layernorm(x + _L0_xattn_ref(x, ctx_4096, ctx_4096, mask_BxSxS2_ff1, L0_xattn_wq, L0_xattn_wk, L0_xattn_wv, L0_xattn_wo), axis=-1)
    x = _layernorm(x + _L0_ffn_ref(x, L0_ffn_gate_qweight, L0_ffn_gate_scales, L0_ffn_gate_zeros, L0_ffn_up_qweight, L0_ffn_up_scales, L0_ffn_up_zeros, L0_ffn_down_qweight, L0_ffn_down_scales, L0_ffn_down_zeros), axis=-1)
    return x

_drawn_inputs = setup_inputs


def setup_inputs(seed=0):
    import zlib

    import numpy as np

    out = dict(_drawn_inputs(seed))
    spreads = {}
    factors = {'L0_attn_bq': 5.311, 'L0_attn_bk': 8.0, 'L0_xattn_wq': 2.794, 'L0_xattn_wk': 2.798}
    for name, (base, spread) in spreads.items():
        noise = np.random.default_rng([zlib.crc32(name.encode()), seed]).standard_normal(out[name].shape)
        drawn = base * np.exp(spread * noise) if base else spread * noise
        out[name] = jnp.asarray(drawn.astype(out[name].dtype))
    for name, factor in factors.items():
        out[name] = (out[name] * factor).astype(out[name].dtype)
    return out
```

```python
from contextlib import ExitStack

import numpy as np

import concourse.bass as bass
from concourse import mybir

ALU = mybir.AluOpType
ACT = mybir.ActivationFunctionType
AX_X = mybir.AxisListType.X
F32 = mybir.dt.float32
F16 = mybir.dt.float16
BF16 = mybir.dt.bfloat16
I32 = mybir.dt.int32

P = 128
NB, S, D = 8, 128, 512
T = NB * S
NK = D // P
HALF = 512
NHALF = T // HALF
BH = HALF // S
H1, HD1 = 32, 16
HC = P // HD1
G, QH, DK = 8, 4, 128
INTER, GS, PACK = 1376, 128, 8
NI = -(-INTER // P)
IPAD = NI * P
EPS = 1e-5

E_X = 6
E_W = 8
E_QK = 6
E_V1 = 6
E_P = 8
E_Q2 = 9
E_V2 = 7
E_I = 3
NEG = -(2.0 ** 100)


def decoder_kernel(nc, x, xT, ctxT, mask, wqT, wkT, wvT, woT, bq, bk, bv, bo, xwq, xwk, xwv, xwo,
                   gq, gs, gz, uq, us, uz, dq, ds, dz, ident_d, tri_d, hmask_d, cosq_d, sinq_d, cosk_d,
                   sink_d, shq_d, shz_d, out):
    with ExitStack() as ctx:
        def sem(name):
            return ctx.enter_context(nc.semaphore(name))

        def sb(name, shape, dt, stack=ctx):
            return stack.enter_context(nc.sbuf_tensor(name, shape, dt))

        bank = [ctx.enter_context(nc.psum_tensor(f"bank{i}", [P, 512], F32)) for i in range(8)]

        res = sb("res", [P, NB, D], F32)
        aTh = sb("aTh", [P, NK, T], F16)
        aTl = sb("aTl", [P, NK, T], F16)
        cTh = sb("cTh", [P, NK, T], F16)
        cTl = sb("cTl", [P, NK, T], F16)
        prob = sb("prob", [P, 2, 512], F32)
        pTh = sb("pTh", [P, 2, 512], F16)
        pTl = sb("pTl", [P, 2, 512], F16)
        nmax = sb("nmax", [P, 2, 4], F32)
        ebias = sb("ebias", [P, 2, 4], F32)
        ident = sb("ident", [P, P], F32)
        identb = sb("identb", [P, P], BF16)
        tri = sb("tri", [P, P], BF16)
        mbias = sb("mbias", [P, NB, S], BF16)
        hmask = sb("hmask", [P, HC], F32)
        bcol = sb("bcol", [P, 3, NK], F32)
        bcols = sb("bcols", [P, 3, NK], F32)
        bnow = sb("bnow", [P, 3], F32)
        cosq = sb("cosq", [P, S], F32)
        sinq = sb("sinq", [P, S], F32)
        cosk = sb("cosk", [P, S], F32)
        sink = sb("sink", [P, S], F32)
        shq = sb("shq", [P, 1], I32)
        shz = sb("shz", [P, PACK], I32)
        lnst = sb("lnst", [P, 2, 6], F32)
        lnmv = sb("lnmv", [P, 2, 2], F32)
        lnsd = sb("lnsd", [P, 2, 2], F32)

        s1 = ExitStack()
        stT = sb("stT", [P, NK, T], F32, s1)
        tri_f = sb("tri_f", [P, P], F32, s1)
        mask_f = sb("mask_f", [P, NB, S], F32, s1)
        bo_bc = sb("bo_bc", [P, D], F32, s1)
        w1s = sb("w1s", [P, 3, NK, P], F32, s1)
        w1h = sb("w1h", [P, 3, NK, P], F16, s1)
        w1l = sb("w1l", [P, 3, NK, P], F16, s1)
        qkf = sb("qkf", [P, 2, HALF], F32, s1)
        q1h = sb("q1h", [P, HALF], F16, s1)
        q1l = sb("q1l", [P, HALF], F16, s1)
        k1h = sb("k1h", [P, HALF], F16, s1)
        k1l = sb("k1l", [P, HALF], F16, s1)
        kmh = sb("kmh", [P, HC, HALF], F16, s1)
        kml = sb("kml", [P, HC, HALF], F16, s1)
        v1h = sb("v1h", [P, BH, HC, HD1 + 1], F16, s1)
        v1l = sb("v1l", [P, BH, HC, HD1], F16, s1)
        onrm = sb("onrm", [P, 2, P], F32, s1)
        rden1 = sb("rden1", [P, 2, HC], F32, s1)
        oTh = sb("oTh", [P, NK, T], F16, s1)
        oTl = sb("oTl", [P, NK, T], F16, s1)
        woTs = sb("woTs", [P, NK, D], F32, s1)
        woTh = sb("woTh", [P, NK, D], F16, s1)
        woTl = sb("woTl", [P, NK, D], F16, s1)
        s1.close()

        s2 = ExitStack()
        xqs = sb("xqs", [P, NK, QH * DK], F32, s2)
        xks = sb("xks", [P, NK, DK], F32, s2)
        xvs = sb("xvs", [P, NK, DK], F32, s2)
        xos = sb("xos", [P, QH, D], F32, s2)
        xqh = sb("xqh", [P, NK, QH * DK], F16, s2)
        xql = sb("xql", [P, NK, QH * DK], F16, s2)
        xkh = sb("xkh", [P, NK, DK], F16, s2)
        xkl = sb("xkl", [P, NK, DK], F16, s2)
        xvh = sb("xvh", [P, NK, DK], F16, s2)
        xvl = sb("xvl", [P, NK, DK], F16, s2)
        xoh = sb("xoh", [P, QH, D], F16, s2)
        xol = sb("xol", [P, QH, D], F16, s2)
        rawt = sb("rawt", [P, 2, HALF], F32, s2)
        rcos = sb("rcos", [P, 2, HALF], F32, s2)
        rsin = sb("rsin", [P, 2, HALF], F32, s2)
        q2h = sb("q2h", [P, NHALF, QH, HALF], F16, s2)
        q2l = sb("q2l", [P, NHALF, QH, HALF], F16, s2)
        k2h = sb("k2h", [P, NHALF, HALF], F16, s2)
        k2l = sb("k2l", [P, NHALF, HALF], F16, s2)
        v2h = sb("v2h", [P, NB, DK], F16, s2)
        v2l = sb("v2l", [P, NB, DK], F16, s2)
        den2 = sb("den2", [P, 2, QH], F32, s2)
        rden2 = sb("rden2", [P, 2, QH], F32, s2)
        pnrm = sb("pnrm", [P, 2, 512], F32, s2)
        o2h = sb("o2h", [P, 2, QH, S], F16, s2)
        o2l = sb("o2l", [P, 2, QH, S], F16, s2)
        s2.close()

        s3 = ExitStack()
        wdh = sb("wdh", [P, NI, D], F16, s3)
        wdl = sb("wdl", [P, NI, D], F16, s3)
        inh = sb("inh", [P, NI, T], F16, s3)
        inl = sb("inl", [P, NI, T], F16, s3)
        qst = sb("qst", [P, 3, 512], I32, s3)
        sst = sb("sst", [P, 3, 512], F16, s3)
        zst = sb("zst", [P, 3, 512 // PACK], I32, s3)
        nib = sb("nib", [P, 512], I32, s3)
        znb = sb("znb", [P, 512], I32, s3)
        dif = sb("dif", [P, 512], F32, s3)
        deq = sb("deq", [P, 3, 512], F32, s3)
        wgh = sb("wgh", [P, 2, 512], F16, s3)
        wgl = sb("wgl", [P, 2, 512], F16, s3)
        sig = sb("sig", [P, NHALF, HALF], F32, s3)
        gated = sb("gated", [P, NHALF, HALF], F32, s3)
        yh = sb("yh", [P, 2, D], F16, s3)
        s3.close()

        const_in, act_in, w1_in, wo1_in = sem("const_in"), sem("act_in"), sem("w1_in"), sem("wo1_in")
        xT_hi, xT_lo, cT_hi, cT_lo = sem("xT_hi"), sem("xT_lo"), sem("cT_hi"), sem("cT_lo")
        consts_ready, res_ready = sem("consts_ready"), sem("res_ready")
        scaled_bias, bias_now, wo1_hi, wo1_ready = sem("scaled_bias"), sem("bias_now"), sem("wo1_hi"), sem("wo1_ready")
        w1_hi, w1_lo = sem("w1_hi"), sem("w1_lo")
        k1_psum, q1_psum, v1_psum = sem("k1_psum"), sem("q1_psum"), sem("v1_psum")
        k1_f32, q1_f32, v1_hi, v1_lo = sem("k1_f32"), sem("q1_f32"), sem("v1_hi"), sem("v1_lo")
        qk_hi, qk_lo, km_ready = sem("qk_hi"), sem("qk_lo"), sem("km_ready")
        s_psum, nmax_done, ebias_done, exp_done = sem("s_psum"), sem("nmax_done"), sem("ebias_done"), sem("exp_done")
        t_psum, pT_hi, pT_lo = sem("t_psum"), sem("pT_hi"), sem("pT_lo")
        pv_done, rden_done, onrm_done, oT_psum = sem("pv_done"), sem("rden_done"), sem("onrm_done"), sem("oT_psum")
        oT_hi, oT_lo = sem("oT_hi"), sem("oT_lo")
        y_psum, ln_sum, ln_stat, ln_mv = sem("y_psum"), sem("ln_sum"), sem("ln_stat"), sem("ln_mv")
        ln_sd, ln_rs, ln_out = sem("ln_sd"), sem("ln_rs"), sem("ln_out")
        xt_psum, xt_hi, xt_lo = sem("xt_psum"), sem("xt_hi"), sem("xt_lo")

        x2_in, x2_hi, x2_lo = sem("x2_in"), sem("x2_hi"), sem("x2_lo")
        tile_psum, tile_raw, tile_cos, tile_sin = sem("tile_psum"), sem("tile_raw"), sem("tile_cos"), sem("tile_sin")
        tile_rot, tile_hi, tile_lo = sem("tile_rot"), sem("tile_hi"), sem("tile_lo")
        v2_psum, v2_hi, v2_lo = sem("v2_psum"), sem("v2_hi"), sem("v2_lo")
        c_s, c_nmax, c_ebias, c_exp = sem("c_s"), sem("c_nmax"), sem("c_ebias"), sem("c_exp")
        c_rden, c_pnrm, c_t, c_pT_hi, c_pT_lo = sem("c_rden"), sem("c_pnrm"), sem("c_t"), sem("c_pT_hi"), sem("c_pT_lo")
        c_pv, c_o_hi, c_o_lo, c_wo, c_acc = sem("c_pv"), sem("c_o_hi"), sem("c_o_lo"), sem("c_wo"), sem("c_acc")

        f_in, f_nib, f_zsh, f_znb, f_dif, f_deq = sem("f_in"), sem("f_nib"), sem("f_zsh"), sem("f_znb"), sem("f_dif"), sem("f_deq")
        f_whi, f_wlo, f_dhi, f_dlo = sem("f_whi"), sem("f_wlo"), sem("f_dhi"), sem("f_dlo")
        f_gate, f_up, f_sig, f_gated, f_inter, f_ihi, f_ilo = (
            sem("f_gate"), sem("f_up"), sem("f_sig"), sem("f_gated"), sem("f_inter"), sem("f_ihi"), sem("f_ilo"))
        f_y, f_y16, out_done = sem("f_y"), sem("f_y16"), sem("out_done")

        NCONST = 16
        UB = 2 * BH
        UC = NHALF * UB
        TILES = NHALF * (1 + QH)

        def split_products(pe, out_ap, ah, al, bh, bl, first, last):
            pe.matmul(out_ap, ah, bh, start=first, stop=False)
            pe.matmul(out_ap, ah, bl, start=False, stop=False)
            return pe.matmul(out_ap, al, bh, start=False, stop=last)

        block = ctx.enter_context(nc.Block())

        @block.sync
        def _(sp):
            sp.dma_start(stT[:, :, :], xT.rearrange("(k p) t -> p k t", p=P)).then_inc(act_in, 16)
            consts = [(ident, ident_d), (tri_f, tri_d), (hmask, hmask_d), (cosq, cosq_d), (sinq, sinq_d),
                      (cosk, cosk_d), (sink, sink_d), (shq, shq_d), (shz, shz_d)]
            with nc.allow_non_contiguous_dma("bias columns"):
                for dst, src in consts:
                    sp.dma_start(dst[:, :], src).then_inc(const_in, 16)
                for i, src in enumerate((bq, bk, bv)):
                    sp.dma_start(bcol[:, i, :], src.rearrange("(c p) -> p c", p=P)).then_inc(const_in, 16)
                sp.dma_start(bo_bc[:, :], bo.partition_broadcast(P)).then_inc(const_in, 16)
                sp.dma_start(mask_f[:, :, :], mask.rearrange("b q k -> q b k")).then_inc(const_in, 16)
                sp.dma_start(res[:, :, :], x.rearrange("b t d -> t b d")).then_inc(const_in, 16)
                sp.dma_start(woTs[:, :, :], woT.rearrange("(k p) n -> p k n", p=P)).then_inc(const_in, 16)
            with sp.Fori(0, NK) as c:
                sp.wait_ge(w1_lo, c * 3)
                for i, w in enumerate((wqT, wkT, wvT)):
                    sp.dma_start(w1s[:, i, :, :],
                                 w.rearrange("(k p) n -> p k n", p=P)[:, :, bass.ds(c * P, P)]).then_inc(w1_in, 16)
            sp.wait_ge(xT_lo, NK)
            sp.dma_start(stT[:, :, :], ctxT.rearrange("(k p) t -> p k t", p=P)).then_inc(act_in, 16)

            sp.wait_ge(xt_lo, NB)
            with sp.Fori(0, G) as g:
                sp.wait_ge(x2_lo, g * 4)
                sp.dma_start(xks[:, :, :], xwk.rearrange("(k p) n -> p k n", p=P)[:, :, bass.ds(g * DK, DK)]).then_inc(x2_in, 16)
                sp.dma_start(xqs[:, :, :], xwq.rearrange("(k p) n -> p k n", p=P)[:, :, bass.ds(g * QH * DK, QH * DK)]).then_inc(x2_in, 16)
                sp.dma_start(xvs[:, :, :], xwv.rearrange("(k p) n -> p k n", p=P)[:, :, bass.ds(g * DK, DK)]).then_inc(x2_in, 16)
                sp.dma_start(xos[:, :, :], xwo.rearrange("(h p) n -> p h n", p=P)[:, bass.ds(g * QH, QH), :]).then_inc(x2_in, 16)

            sp.wait_ge(xt_lo, 2 * NB)
            with sp.Fori(0, NI) as i:
                sp.wait_ge(f_deq, i * 3)
                for m, (qw, sc, zw) in enumerate(((gq, gs, gz), (uq, us, uz), (dq, ds, dz))):
                    sp.dma_start(qst[:, m, :], qw[i]).then_inc(f_in, 16)
                    sp.dma_start(sst[:, m, :], sc[i].partition_broadcast(P)).then_inc(f_in, 16)
                    sp.dma_start(zst[:, m, :], zw[i].partition_broadcast(P)).then_inc(f_in, 16)
            for b in range(NB):
                sp.wait_ge(ln_out, 2 * NB + b + 1)
                sp.dma_start(out[b], res[:, b, :]).then_inc(out_done, 16)
            sp.wait_ge(out_done, 16 * NB)

        @block.gpsimd
        def _(pool):
            pool.wait_ge(const_in, 16 * NCONST)
            nc.gpsimd.tensor_copy(identb[:, :], ident[:, :]).then_inc(consts_ready, 1)
            nc.gpsimd.tensor_copy(tri[:, :], tri_f[:, :]).then_inc(consts_ready, 1)
            for b in range(NB):
                nc.gpsimd.tensor_tensor(res[:, b, :], res[:, b, :], bo_bc[:, :], ALU.add).then_inc(res_ready, 1)

            def by_batch(table):
                return table[:, :].unsqueeze(1).to_broadcast([P, BH, S])

            def as_batches(tile):
                return tile.rearrange("p (b t) -> p b t", b=BH)

            with pool.Fori(0, G) as g:
                def rotate(n, table):
                    i = n % 2
                    pool.wait_ge(tile_raw, g * TILES + n + 1)
                    nc.gpsimd.tensor_tensor(as_batches(rcos[:, i, :]), as_batches(rawt[:, i, :]), by_batch(table),
                                            ALU.mult).then_inc(tile_cos, 1)
                    pool.wait_ge(tile_cos, g * TILES + n + 1)
                    pool.wait_ge(tile_sin, g * TILES + n + 1)
                    nc.gpsimd.tensor_tensor(rcos[:, i, :], rcos[:, i, :], rsin[:, i, :], ALU.add).then_inc(tile_rot, 1)

                for half in range(NHALF):
                    for n in range(1 + QH):
                        rotate(half * (1 + QH) + n, cosk if n == 0 else cosq)

        @block.scalar
        def _(act):
            def split_hi(dst, src, e):
                return nc.scalar.activation(dst, src, ACT.Copy, scale=2.0 ** e)

            act.wait_ge(act_in, 16)
            for k in range(NK):
                split_hi(aTh[:, k, :], stT[:, k, :], E_X).then_inc(xT_hi, 1)
            act.wait_ge(const_in, 16 * NCONST)
            for i, e in enumerate((E_QK, E_QK, E_V1)):
                split_hi(bcols[:, i, :], bcol[:, i, :], e).then_inc(scaled_bias, 1)
            for k in range(NK):
                split_hi(woTh[:, k, :], woTs[:, k, :], E_W).then_inc(wo1_hi, 1)

            with act.Fori(0, NK) as c:
                act.wait_ge(w1_in, (c + 1) * 48)
                act.wait_ge(v1_psum, c * NHALF)
                for i in range(3):
                    split_hi(w1h[:, i, :, :], w1s[:, i, :, :], E_W).then_inc(w1_hi, 1)
                for half in range(NHALF):
                    n1 = c * NHALF + half + 1
                    act.wait_ge(k1_psum, n1)
                    act.wait_ge(qk_lo, (n1 - 1) * 2)
                    act.wait_ge(bias_now, c + 1)
                    nc.scalar.activation(qkf[:, 0, :], bank[0][:, :], ACT.Identity, scale=2.0 ** (E_QK - E_X - E_W),
                                         bias=bnow[:, 1:2]).then_inc(k1_f32, 1)
                    act.wait_ge(q1_psum, n1)
                    nc.scalar.activation(qkf[:, 1, :], bank[1][:, :], ACT.Identity, scale=2.0 ** (E_QK - E_X - E_W),
                                         bias=bnow[:, 0:1]).then_inc(q1_f32, 1)
                    act.wait_ge(v1_psum, n1)
                    act.wait_ge(pv_done, (n1 - 1) * UB)
                    nc.scalar.activation(v1h[:, :, :, 0:HD1],
                                         bank[7][:, :].rearrange("p (b h d) -> p b h d", b=BH, h=HC),
                                         ACT.Copy, scale=2.0 ** (E_V1 - E_X - E_W)).then_inc(v1_hi, 1)

                    def base(n):
                        return c * UC + half * UB + n

                    def exps(n):
                        act.wait_ge(ebias_done, base(n) + 1)
                        if n >= 2:
                            act.wait_ge(t_psum, base(n) - 1)
                        for j in range(4):
                            last = nc.scalar.activation(prob[:, n % 2, j * S:(j + 1) * S],
                                                        bank[2 + n % 2][:, j * S:(j + 1) * S], ACT.Exp,
                                                        bias=ebias[:, n % 2, j:j + 1], scale=2.0 ** (-2 * E_QK) / 4)
                        last.then_inc(exp_done, 1)

                    def p_hi(n):
                        act.wait_ge(t_psum, base(n) + 1)
                        if n >= 2:
                            act.wait_ge(pv_done, base(n) - 1)
                        split_hi(pTh[:, n % 2, :], bank[4][:, :], E_P).then_inc(pT_hi, 1)

                    for n in range(UB + 1):
                        if n < UB:
                            exps(n)
                        if n >= 1:
                            p_hi(n - 1)

            def layer_norm_tail(first, stage):
                for b in range(NB):
                    act.wait_ge(ln_mv, first + b + 1)
                    nc.scalar.activation(lnsd[:, b % 2, 0:1], lnmv[:, b % 2, 1:2], ACT.Sqrt).then_inc(ln_sd, 1)
                    if stage:
                        act.wait_ge(xt_psum, first + b + 1)
                        split_hi(aTh[:, :, b * S:(b + 1) * S], bank[2 + b % 2][:, :].rearrange("p (k t) -> p k t", k=NK),
                                 E_X).then_inc(xt_hi, 1)

            act.wait_ge(act_in, 32)
            for k in range(NK):
                split_hi(cTh[:, k, :], stT[:, k, :], E_X).then_inc(cT_hi, 1)
            layer_norm_tail(0, True)

            with act.Fori(0, G) as g:
                act.wait_ge(x2_in, (g + 1) * 64)
                act.wait_ge(c_wo, g * NB)
                for dst, src in ((xkh, xks), (xqh, xqs), (xvh, xvs), (xoh, xos)):
                    split_hi(dst[:, :, :], src[:, :, :], E_W).then_inc(x2_hi, 1)

                def raw_tile(n, e):
                    act.wait_ge(tile_psum, g * TILES + n + 1)
                    if n >= 2:
                        act.wait_ge(tile_rot, g * TILES + n - 1)
                    nc.scalar.activation(rawt[:, n % 2, :], bank[n % 2][:, :], ACT.Copy,
                                         scale=2.0 ** (e - E_X - E_W)).then_inc(tile_raw, 1)

                def attend(u):
                    def exps(n):
                        act.wait_ge(c_ebias, g * NB + n + 1)
                        if n >= 2:
                            act.wait_ge(c_pnrm, g * NB + n - 1)
                        for j in range(QH):
                            last = nc.scalar.activation(prob[:, n % 2, j * S:(j + 1) * S],
                                                        bank[2 + n % 2][:, j * S:(j + 1) * S], ACT.Exp,
                                                        bias=ebias[:, n % 2, j:j + 1], scale=2.0 ** (-E_QK - E_Q2),
                                                        accum_out=den2[:, n % 2, j:j + 1])
                        last.then_inc(c_exp, 1)

                    def p_hi(n):
                        act.wait_ge(c_t, g * NB + n + 1)
                        if n >= 2:
                            act.wait_ge(c_pv, g * NB + n - 1)
                        split_hi(pTh[:, n % 2, :], bank[4][:, :], E_P).then_inc(c_pT_hi, 1)

                    def o_hi(n):
                        act.wait_ge(c_pv, g * NB + n + 1)
                        if n >= 2:
                            act.wait_ge(c_wo, g * NB + n - 1)
                        split_hi(o2h[:, n % 2, :, :], bank[5][:, :].rearrange("p (h t) -> p h t", h=QH),
                                 E_V2 - E_P - E_V2).then_inc(c_o_hi, 1)

                    if u < NB:
                        exps(u)
                    if 1 <= u <= NB:
                        p_hi(u - 1)
                    if 2 <= u <= NB + 1:
                        o_hi(u - 2)

                for half in range(NHALF):
                    for n in range(1 + QH):
                        raw_tile(half * (1 + QH) + n, E_QK if n == 0 else E_Q2)
                    act.wait_ge(v2_psum, g * NHALF + half + 1)
                    split_hi(v2h[:, half * BH:(half + 1) * BH, :], bank[6 + half][:, :].rearrange("p (b d) -> p b d", b=BH),
                             E_V2 - E_X - E_W).then_inc(v2_hi, 1)
                for u in range(NB + 2):
                    attend(u)
            layer_norm_tail(NB, True)

            with act.Fori(0, NI) as i:
                for m in range(2):
                    act.wait_ge(f_deq, i * 3 + m + 1)
                    act.wait_ge(f_up if m else f_gate, i * NHALF)
                    split_hi(wgh[:, m, :], deq[:, m, :], E_W).then_inc(f_whi, 1)
                for half in range(NHALF):
                    act.wait_ge(f_gate, i * NHALF + half + 1)
                    act.wait_ge(f_gated, i * NHALF + half)
                    nc.scalar.activation(sig[:, half, :], bank[2 * half][:, :], ACT.Sigmoid,
                                         scale=2.0 ** (-E_X - E_W)).then_inc(f_sig, 1)
            layer_norm_tail(2 * NB, False)

        @block.vector
        def _(dve):
            def split_lo(dst, src, hi, e):
                return nc.vector.scalar_tensor_tensor(out=dst, in0=src, scalar=2.0 ** e, in1=hi,
                                                      op0=ALU.mult, op1=ALU.subtract)

            nc.vector.memset(v1h[:, :, :, HD1:HD1 + 1], 1.0).then_inc(consts_ready, 1)
            for k in range(NK):
                dve.wait_ge(xT_hi, k + 1)
                split_lo(aTl[:, k, :], stT[:, k, :], aTh[:, k, :], E_X).then_inc(xT_lo, 1)
            dve.wait_ge(const_in, 16 * NCONST)
            nc.vector.tensor_scalar(mbias[:, :, :], mask_f[:, :, :], 0.0, NEG, ALU.is_equal,
                                    ALU.mult).then_inc(consts_ready, 1)
            for k in range(NK):
                dve.wait_ge(wo1_hi, k + 1)
                split_lo(woTl[:, k, :], woTs[:, k, :], woTh[:, k, :], E_W).then_inc(wo1_ready, 1)

            dve.wait_ge(scaled_bias, 3)
            with dve.Fori(0, NK) as c:
                dve.wait_ge(q1_f32, c * NHALF)
                dve.wait_ge(oT_lo, c * NHALF)
                nc.vector.tensor_scalar(bnow[:, :].unsqueeze(2), bcols[:, :, bass.ds(c, 1)], 1.0, None,
                                        ALU.mult).then_inc(bias_now, 1)
                dve.wait_ge(v1_psum, c * NHALF)
                for i in range(3):
                    dve.wait_ge(w1_hi, c * 3 + i + 1)
                    split_lo(w1l[:, i, :, :], w1s[:, i, :, :], w1h[:, i, :, :], E_W).then_inc(w1_lo, 1)
                for half in range(NHALF):
                    n1 = c * NHALF + half + 1
                    for i, (ready, hi, lo) in enumerate(((k1_f32, k1h, k1l), (q1_f32, q1h, q1l))):
                        dve.wait_ge(ready, n1)
                        dve.wait_ge(s_psum, (n1 - 1) * UB)
                        nc.vector.tensor_copy(hi[:, :], qkf[:, i, :]).then_inc(qk_hi, 1)
                        dve.wait_ge(qk_hi, (n1 - 1) * 2 + i + 1)
                        nc.vector.tensor_tensor(lo[:, :], qkf[:, i, :], hi[:, :], ALU.subtract).then_inc(qk_lo, 1)
                    dve.wait_ge(qk_lo, n1 * 2)
                    for m in range(HC):
                        nc.vector.tensor_scalar(kmh[:, m, :], k1h[:, :], hmask[:, m:m + 1], None, ALU.mult)
                        last = nc.vector.tensor_scalar(kml[:, m, :], k1l[:, :], hmask[:, m:m + 1], None, ALU.mult)
                    last.then_inc(km_ready, 1)
                    dve.wait_ge(v1_hi, n1)
                    dve.wait_ge(pv_done, (n1 - 1) * UB)
                    psum_v = bank[7][:, :].rearrange("p (b h d) -> p (b h) d", b=BH, h=HC)
                    split_lo(v1l[:, :, :, :].rearrange("p b h d -> p (b h) d"), psum_v,
                             v1h[:, :, :, :].rearrange("p b h d -> p (b h) d")[:, :, 0:HD1],
                             E_V1 - E_X - E_W).then_inc(v1_lo, 1)

                    def base(n):
                        return c * UC + half * UB + n

                    def row_max(n):
                        dve.wait_ge(s_psum, base(n) + 1)
                        if n >= 2:
                            dve.wait_ge(exp_done, base(n) - 1)
                        nc.vector.tensor_reduce(nmax[:, n % 2, :], bank[2 + n % 2][:, :].rearrange("p (h k) -> p h k", h=4),
                                                AX_X, ALU.max, negate=True).then_inc(nmax_done, 1)
                        dve.wait_ge(nmax_done, base(n) + 1)
                        nc.vector.tensor_scalar(ebias[:, n % 2, :], nmax[:, n % 2, :], 2.0 ** (-2 * E_QK) / 4, None,
                                                ALU.mult).then_inc(ebias_done, 1)

                    def p_lo(n):
                        dve.wait_ge(pT_hi, base(n) + 1)
                        if n >= 2:
                            dve.wait_ge(pv_done, base(n) - 1)
                        split_lo(pTl[:, n % 2, :], bank[4][:, :], pTh[:, n % 2, :], E_P).then_inc(pT_lo, 1)

                    def normalise(b):
                        nb = (n1 - 1) * BH + b
                        dve.wait_ge(pv_done, (n1 - 1) * UB + 2 * b + 2)
                        if b >= 2:
                            dve.wait_ge(oT_psum, nb - 1)
                        o = bank[5][:, 0:HC * (HD1 + 1)].rearrange("p (h d) -> p h d", h=HC)
                        nc.vector.reciprocal(rden1[:, b % 2, :].unsqueeze(2), o[:, :, HD1:HD1 + 1]).then_inc(rden_done, 1)
                        dve.wait_ge(rden_done, nb + 1)
                        nc.vector.tensor_tensor(onrm[:, b % 2, :].rearrange("p (h d) -> p h d", h=HC), o[:, :, 0:HD1],
                                                rden1[:, b % 2, :].unsqueeze(2).to_broadcast([P, HC, HD1]),
                                                ALU.mult).then_inc(onrm_done, 1)

                    for n in range(UB + 2):
                        if n < UB:
                            row_max(n)
                        if 1 <= n <= UB:
                            p_lo(n - 1)
                        if n >= 3 and n % 2 == 1:
                            normalise((n - 3) // 2)
                    dve.wait_ge(oT_psum, n1 * BH)
                    nc.vector.tensor_scalar(oTh[:, bass.ds(c, 1), half * HALF:(half + 1) * HALF],
                                            bank[6][:, :].unsqueeze(1), bnow[:, 2:3], None, ALU.add).then_inc(oT_hi, 1)
                    dve.wait_ge(oT_hi, n1)
                    nc.vector.scalar_tensor_tensor(
                        out=oTl[:, bass.ds(c, 1), half * HALF:(half + 1) * HALF], in0=bank[6][:, :].unsqueeze(1),
                        scalar=bnow[:, 2:3], in1=oTh[:, bass.ds(c, 1), half * HALF:(half + 1) * HALF],
                        op0=ALU.add, op1=ALU.subtract).then_inc(oT_lo, 1)

            for k in range(NK):
                dve.wait_ge(cT_hi, k + 1)
                split_lo(cTl[:, k, :], stT[:, k, :], cTh[:, k, :], E_X).then_inc(cT_lo, 1)

            def layer_norm(first, add_psum, stage):
                for b in range(NB):
                    i = b % 2
                    r = res[:, b, :]
                    done = first + b + 1
                    if add_psum:
                        add_psum(b)
                    nc.vector.bn_stats(lnst[:, i, :], r).then_inc(ln_stat, 1)
                    dve.wait_ge(ln_stat, done)
                    nc.vector.bn_aggr(lnmv[:, i, :], lnst[:, i, :]).then_inc(ln_rs, 1)
                    dve.wait_ge(ln_rs, 3 * (done - 1) + 1)
                    nc.vector.tensor_scalar(lnmv[:, i, 1:2], lnmv[:, i, 1:2], EPS, None, ALU.add).then_inc(ln_mv, 1)
                    dve.wait_ge(ln_sd, done)
                    nc.vector.reciprocal(lnsd[:, i, 1:2], lnsd[:, i, 0:1]).then_inc(ln_rs, 1)
                    dve.wait_ge(ln_rs, 3 * (done - 1) + 2)
                    dve.wait_ge(ln_mv, done)
                    nc.vector.tensor_scalar(r, r, lnmv[:, i, 0:1], lnsd[:, i, 1:2], ALU.subtract,
                                            ALU.mult).then_inc(ln_out, 1)
                    dve.wait_ge(ln_out, done)
                    nc.vector.tensor_copy(lnst[:, i, 0:1], lnsd[:, i, 1:2]).then_inc(ln_rs, 1)
                    dve.wait_ge(ln_rs, 3 * done)
                    if stage:
                        dve.wait_ge(xt_hi, done)
                        split_lo(aTl[:, :, b * S:(b + 1) * S], bank[2 + i][:, :].rearrange("p (k t) -> p k t", k=NK),
                                 aTh[:, :, b * S:(b + 1) * S], E_X).then_inc(xt_lo, 1)

            def add_self(b):
                dve.wait_ge(y_psum, b + 1)
                dve.wait_ge(res_ready, b + 1)
                nc.vector.scalar_tensor_tensor(out=res[:, b, :], in0=bank[b % 2][:, :], scalar=2.0 ** (-E_V1 - E_W),
                                               in1=res[:, b, :], op0=ALU.mult, op1=ALU.add).then_inc(ln_sum, 1)
                dve.wait_ge(ln_sum, b + 1)

            layer_norm(0, add_self, True)

            with dve.Fori(0, G) as g:
                dve.wait_ge(c_wo, g * NB)
                for n, (dst, src, hi) in enumerate(((xkl, xks, xkh), (xql, xqs, xqh), (xvl, xvs, xvh), (xol, xos, xoh))):
                    dve.wait_ge(x2_hi, g * 4 + n + 1)
                    split_lo(dst[:, :, :], src[:, :, :], hi[:, :, :], E_W).then_inc(x2_lo, 1)

                def rotate(n, dst_h, dst_l, table):
                    i = n % 2
                    dve.wait_ge(tile_raw, g * TILES + n + 1)
                    if n >= 2:
                        dve.wait_ge(tile_rot, g * TILES + n - 1)
                    lo, hi = slice(0, P // 2), slice(P // 2, P)
                    for dst, src in ((lo, hi), (hi, lo)):
                        last = nc.vector.tensor_tensor(
                            rsin[dst, i, :].rearrange("p (b t) -> p b t", b=BH),
                            rawt[src, i, :].rearrange("p (b t) -> p b t", b=BH),
                            table[src, :].unsqueeze(1).to_broadcast([P // 2, BH, S]), ALU.mult)
                    last.then_inc(tile_sin, 1)
                    dve.wait_ge(tile_rot, g * TILES + n + 1)
                    nc.vector.tensor_copy(dst_h, rcos[:, i, :]).then_inc(tile_hi, 1)
                    dve.wait_ge(tile_hi, g * TILES + n + 1)
                    nc.vector.tensor_tensor(dst_l, rcos[:, i, :], dst_h, ALU.subtract).then_inc(tile_lo, 1)

                for half in range(NHALF):
                    rotate(half * (1 + QH), k2h[:, half, :], k2l[:, half, :], sink)
                    for h in range(QH):
                        rotate(half * (1 + QH) + 1 + h, q2h[:, half, h, :], q2l[:, half, h, :], sinq)
                    dve.wait_ge(v2_hi, g * NHALF + half + 1)
                    split_lo(v2l[:, half * BH:(half + 1) * BH, :], bank[6 + half][:, :].rearrange("p (b d) -> p b d", b=BH),
                             v2h[:, half * BH:(half + 1) * BH, :], E_V2 - E_X - E_W).then_inc(v2_lo, 1)

                def row_max(n):
                    dve.wait_ge(c_s, g * NB + n + 1)
                    if n >= 2:
                        dve.wait_ge(c_exp, g * NB + n - 1)
                    nc.vector.tensor_reduce(nmax[:, n % 2, :], bank[2 + n % 2][:, :].rearrange("p (h k) -> p h k", h=QH),
                                            AX_X, ALU.max, negate=True).then_inc(c_nmax, 1)
                    dve.wait_ge(c_nmax, g * NB + n + 1)
                    nc.vector.tensor_scalar(ebias[:, n % 2, :], nmax[:, n % 2, :], 2.0 ** (-E_QK - E_Q2), None,
                                            ALU.mult).then_inc(c_ebias, 1)

                def p_norm(n):
                    dve.wait_ge(c_exp, g * NB + n + 1)
                    nc.vector.reciprocal(rden2[:, n % 2, :], den2[:, n % 2, :]).then_inc(c_rden, 1)
                    dve.wait_ge(c_rden, g * NB + n + 1)
                    if n >= 2:
                        dve.wait_ge(c_t, g * NB + n - 1)
                    nc.vector.tensor_tensor(pnrm[:, n % 2, :].rearrange("p (h k) -> p h k", h=QH),
                                            prob[:, n % 2, :].rearrange("p (h k) -> p h k", h=QH),
                                            rden2[:, n % 2, :].unsqueeze(2).to_broadcast([P, QH, S]),
                                            ALU.mult).then_inc(c_pnrm, 1)

                def p_lo(n):
                    dve.wait_ge(c_pT_hi, g * NB + n + 1)
                    if n >= 2:
                        dve.wait_ge(c_pv, g * NB + n - 1)
                    split_lo(pTl[:, n % 2, :], bank[4][:, :], pTh[:, n % 2, :], E_P).then_inc(c_pT_lo, 1)

                def o_lo(n):
                    dve.wait_ge(c_o_hi, g * NB + n + 1)
                    if n >= 2:
                        dve.wait_ge(c_wo, g * NB + n - 1)
                    split_lo(o2l[:, n % 2, :, :], bank[5][:, :].rearrange("p (h t) -> p h t", h=QH), o2h[:, n % 2, :, :],
                             -E_P).then_inc(c_o_lo, 1)

                def add_out(n):
                    dve.wait_ge(c_wo, g * NB + n + 1)
                    nc.vector.scalar_tensor_tensor(out=res[:, n, :], in0=bank[6 + n % 2][:, :], scalar=2.0 ** (-E_V2 - E_W),
                                                   in1=res[:, n, :], op0=ALU.mult, op1=ALU.add).then_inc(c_acc, 1)

                for n in range(NB + 3):
                    if n < NB:
                        row_max(n)
                        p_norm(n)
                    if 1 <= n <= NB:
                        p_lo(n - 1)
                    if 2 <= n <= NB + 1:
                        o_lo(n - 2)
                    if n >= 3:
                        add_out(n - 3)

            dve.wait_ge(c_acc, G * NB)
            layer_norm(NB, None, True)

            with dve.Fori(0, NI) as i:
                for m in range(3):
                    done = i * 3 + m
                    if m == 0:
                        dve.wait_ge(f_in, (i + 1) * 144)
                    nc.vector.tensor_scalar(nib[:, :], qst[:, m, :], shq[:, 0:1], 15, ALU.logical_shift_right,
                                            ALU.bitwise_and).then_inc(f_nib, 1)
                    nc.vector.tensor_tensor(znb[:, :].rearrange("p (w j) -> p w j", j=PACK),
                                            zst[:, m, :].unsqueeze(2).to_broadcast([P, 512 // PACK, PACK]),
                                            shz[:, :].unsqueeze(1).to_broadcast([P, 512 // PACK, PACK]),
                                            ALU.logical_shift_right).then_inc(f_zsh, 1)
                    dve.wait_ge(f_zsh, done + 1)
                    nc.vector.tensor_scalar(znb[:, :], znb[:, :], 15, None, ALU.bitwise_and).then_inc(f_znb, 1)
                    dve.wait_ge(f_nib, done + 1)
                    dve.wait_ge(f_znb, done + 1)
                    nc.vector.tensor_tensor(dif[:, :], nib[:, :], znb[:, :], ALU.subtract).then_inc(f_dif, 1)
                    dve.wait_ge(f_dif, done + 1)
                    dve.wait_ge(f_wlo if m < 2 else f_dlo, (i * 2 + m) if m < 2 else i)
                    nc.vector.scalar_tensor_tensor(out=deq[:, m, :], in0=dif[:, :], scalar=-1.0, in1=sst[:, m, :],
                                                   op0=ALU.add, op1=ALU.mult).then_inc(f_deq, 1)
                    dve.wait_ge(f_deq, done + 1)
                    if m < 2:
                        dve.wait_ge(f_whi, i * 2 + m + 1)
                        split_lo(wgl[:, m, :], deq[:, m, :], wgh[:, m, :], E_W).then_inc(f_wlo, 1)
                    else:
                        nc.vector.tensor_scalar(wdh[:, bass.ds(i, 1), :], deq[:, 2, :].unsqueeze(1), 2.0 ** E_W, None,
                                                ALU.mult).then_inc(f_dhi, 1)
                        dve.wait_ge(f_dhi, i + 1)
                        split_lo(wdl[:, bass.ds(i, 1), :], deq[:, 2, :].unsqueeze(1), wdh[:, bass.ds(i, 1), :],
                                 E_W).then_inc(f_dlo, 1)
                for half in range(NHALF):
                    n = i * NHALF + half
                    dve.wait_ge(f_sig, n + 1)
                    dve.wait_ge(f_ilo, n)
                    nc.vector.tensor_tensor(gated[:, half, :], bank[2 * half][:, :], sig[:, half, :],
                                            ALU.mult).then_inc(f_gated, 1)
                    dve.wait_ge(f_gated, n + 1)
                    dve.wait_ge(f_up, n + 1)
                    nc.vector.scalar_tensor_tensor(out=gated[:, half, :], in0=bank[2 * half + 1][:, :],
                                                   scalar=2.0 ** (E_I - 2 * E_X - 2 * E_W), in1=gated[:, half, :],
                                                   op0=ALU.mult, op1=ALU.mult).then_inc(f_inter, 1)
                    dve.wait_ge(f_inter, n + 1)
                    nc.vector.tensor_scalar(inh[:, bass.ds(i, 1), half * HALF:(half + 1) * HALF],
                                            gated[:, half, :].unsqueeze(1), 1.0, None, ALU.mult).then_inc(f_ihi, 1)
                    dve.wait_ge(f_ihi, n + 1)
                    nc.vector.tensor_tensor(inl[:, bass.ds(i, 1), half * HALF:(half + 1) * HALF],
                                            gated[:, half, :].unsqueeze(1),
                                            inh[:, bass.ds(i, 1), half * HALF:(half + 1) * HALF],
                                            ALU.subtract).then_inc(f_ilo, 1)

            def add_ffn(b):
                dve.wait_ge(f_y, b + 1)
                nc.vector.tensor_scalar(yh[:, b % 2, :], bank[4 + b % 2][:, :], 2.0 ** (-E_I - E_W), None,
                                        ALU.mult).then_inc(f_y16, 1)
                dve.wait_ge(f_y16, b + 1)
                nc.vector.tensor_tensor(res[:, b, :], res[:, b, :], yh[:, b % 2, :], ALU.add).then_inc(ln_sum, 1)
                dve.wait_ge(ln_sum, NB + b + 1)

            layer_norm(2 * NB, add_ffn, False)

        @block.tensor
        def _(pe):
            pe_ = nc.tensor
            pe.wait_ge(xT_lo, NK)
            pe.wait_ge(consts_ready, 4)

            def project(dst, wh, wl, xh, xl, cols):
                for k in range(NK):
                    last = split_products(pe_, dst, wh[k], wl[k], xh[:, k, cols], xl[:, k, cols], k == 0, k == NK - 1)
                return last

            def project_rows(dst, xh, xl, wh, wl, t0):
                for k in range(NK):
                    last = split_products(pe_, dst, xh[:, k, t0:t0 + S], xl[:, k, t0:t0 + S], wh[k], wl[k],
                                          k == 0, k == NK - 1)
                return last

            with pe.Fori(0, NK) as c:
                pe.wait_ge(w1_lo, (c + 1) * 3)
                for half in range(NHALF):
                    n1 = c * NHALF + half + 1
                    cols = slice(half * HALF, (half + 1) * HALF)
                    pe.wait_ge(q1_f32, n1 - 1)
                    wk = [(w1h[:, 1, k, :], w1l[:, 1, k, :]) for k in range(NK)]
                    project(bank[0][:, :], [a for a, _ in wk], [b for _, b in wk], aTh, aTl, cols).then_inc(k1_psum, 1)
                    wq = [(w1h[:, 0, k, :], w1l[:, 0, k, :]) for k in range(NK)]
                    project(bank[1][:, :], [a for a, _ in wq], [b for _, b in wq], aTh, aTl, cols).then_inc(q1_psum, 1)
                    pe.wait_ge(v1_lo, n1 - 1)
                    for b in range(BH):
                        last = project_rows(bank[7][:, b * P:(b + 1) * P], aTh, aTl, [w1h[:, 2, k, :] for k in range(NK)],
                                            [w1l[:, 2, k, :] for k in range(NK)], half * HALF + b * S)
                    last.then_inc(v1_psum, 1)

                    def base(n):
                        return c * UC + half * UB + n

                    def scores(n):
                        b, heads = n // 2, slice(4 * (n % 2), 4 * (n % 2) + 4)
                        t = slice(b * S, (b + 1) * S)
                        if n == 0:
                            pe.wait_ge(km_ready, n1)
                        if n >= 2:
                            pe.wait_ge(exp_done, base(n) - 1)
                        dst = bank[2 + n % 2][:, :].rearrange("p (h k) -> p h k", h=4)
                        pe_.matmul(dst, identb[:, :], tri[:, :].unsqueeze(1).to_broadcast([P, 4, S]), start=True, stop=False)
                        pe_.matmul(dst, q1h[:, t], kmh[:, heads, t], start=False, stop=False)
                        pe_.matmul(dst, q1h[:, t], kml[:, heads, t], start=False, stop=False)
                        pe_.matmul(dst, q1l[:, t], kmh[:, heads, t], start=False, stop=True).then_inc(s_psum, 1)

                    def turn(n):
                        pe.wait_ge(exp_done, base(n) + 1)
                        pe.wait_ge(pT_lo, base(n))
                        for j in range(4):
                            last = pe_.transpose(bank[4][:, j * S:(j + 1) * S], prob[:, n % 2, j * S:(j + 1) * S], ident[:, :])
                        last.then_inc(t_psum, 1)

                    def weigh(n):
                        b = n // 2
                        pe.wait_ge(pT_lo, base(n) + 1)
                        if n == 0:
                            pe.wait_ge(v1_lo, n1)
                        if n % 2 == 0:
                            pe.wait_ge(onrm_done, (n1 - 1) * BH + b)
                        for j in range(4):
                            h = 4 * (n % 2) + j
                            dst = bank[5][:, h * (HD1 + 1):(h + 1) * (HD1 + 1)]
                            ph, pl = (t[:, n % 2, j * S:(j + 1) * S] for t in (pTh, pTl))
                            pe_.matmul(dst, ph, v1h[:, b, h, :], start=True, stop=False)
                            pe_.matmul(dst[:, 0:HD1], ph, v1l[:, b, h, :], start=False, stop=False)
                            last = pe_.matmul(dst, pl, v1h[:, b, h, :], start=False, stop=True)
                        last.then_inc(pv_done, 1)

                    def turn_out(b):
                        pe.wait_ge(onrm_done, (n1 - 1) * BH + b + 1)
                        if b == 0:
                            pe.wait_ge(oT_lo, n1 - 1)
                        pe_.transpose(bank[6][:, b * S:(b + 1) * S], onrm[:, b % 2, :], ident[:, :]).then_inc(oT_psum, 1)

                    for n in range(UB + 3):
                        if n < UB:
                            scores(n)
                        if 1 <= n <= UB:
                            turn(n - 1)
                        if 2 <= n <= UB + 1:
                            weigh(n - 2)
                        if n >= 4 and n % 2 == 0:
                            turn_out((n - 4) // 2)

            def turn_stream(first, b):
                pe.wait_ge(ln_out, first + b + 1)
                if b >= 2:
                    pe.wait_ge(xt_lo, first + b - 1)
                for k in range(NK):
                    last = pe_.transpose(bank[2 + b % 2][:, k * P:(k + 1) * P], res[:, b, k * P:(k + 1) * P], ident[:, :])
                last.then_inc(xt_psum, 1)

            pe.wait_ge(oT_lo, NK * NHALF)
            pe.wait_ge(wo1_ready, NK)
            for b in range(NB + 1):
                if b < NB:
                    if b >= 2:
                        pe.wait_ge(ln_sum, b - 1)
                    for k in range(NK):
                        last = split_products(pe_, bank[b % 2][:, :], oTh[:, k, b * S:(b + 1) * S],
                                              oTl[:, k, b * S:(b + 1) * S], woTh[:, k, :], woTl[:, k, :], k == 0, k == NK - 1)
                    last.then_inc(y_psum, 1)
                if b >= 1:
                    turn_stream(0, b - 1)

            pe.wait_ge(cT_lo, NK)
            pe.wait_ge(xt_lo, NB)
            with pe.Fori(0, G) as g:
                pe.wait_ge(x2_lo, (g + 1) * 4)
                pe.wait_ge(c_acc, g * NB)

                def rotated(n, dst, wh, wl, xh, xl, cols):
                    if n >= 2:
                        pe.wait_ge(tile_raw, g * TILES + n - 1)
                    project(dst, wh, wl, xh, xl, cols).then_inc(tile_psum, 1)

                for half in range(NHALF):
                    n0 = half * (1 + QH)
                    cols = slice(half * HALF, (half + 1) * HALF)
                    rotated(n0, bank[n0 % 2][:, :], [xkh[:, k, :] for k in range(NK)], [xkl[:, k, :] for k in range(NK)],
                            cTh, cTl, cols)
                    for h in range(QH):
                        f = slice(h * DK, (h + 1) * DK)
                        rotated(n0 + 1 + h, bank[(n0 + 1 + h) % 2][:, :], [xqh[:, k, f] for k in range(NK)],
                                [xql[:, k, f] for k in range(NK)], aTh, aTl, cols)
                    for b in range(BH):
                        last = project_rows(bank[6 + half][:, b * P:(b + 1) * P], cTh, cTl, [xvh[:, k, :] for k in range(NK)],
                                            [xvl[:, k, :] for k in range(NK)], half * HALF + b * S)
                    last.then_inc(v2_psum, 1)

                def scores(n):
                    half, b = n // BH, n % BH
                    t = slice(b * S, (b + 1) * S)
                    if b == 0:
                        pe.wait_ge(tile_lo, g * TILES + (half + 1) * (1 + QH))
                    if n >= 2:
                        pe.wait_ge(c_exp, g * NB + n - 1)
                    full = bank[2 + n % 2]
                    pe_.matmul(full[:, :].rearrange("p (h k) -> p h k", h=QH), identb[:, :],
                               mbias[:, n, :].unsqueeze(1).to_broadcast([P, QH, S]), start=True, stop=False)
                    for h in range(QH):
                        dst = full[:, h * S:(h + 1) * S]
                        pe_.matmul(dst, q2h[:, half, h, t], k2h[:, half, t], start=False, stop=False)
                        pe_.matmul(dst, q2h[:, half, h, t], k2l[:, half, t], start=False, stop=False)
                        last = pe_.matmul(dst, q2l[:, half, h, t], k2h[:, half, t], start=False, stop=(h == QH - 1))
                    last.then_inc(c_s, 1)

                def turn(n):
                    pe.wait_ge(c_pnrm, g * NB + n + 1)
                    pe.wait_ge(c_pT_lo, g * NB + n)
                    for h in range(QH):
                        last = pe_.transpose(bank[4][:, h * S:(h + 1) * S], pnrm[:, n % 2, h * S:(h + 1) * S], ident[:, :])
                    last.then_inc(c_t, 1)

                def weigh(n):
                    pe.wait_ge(c_pT_lo, g * NB + n + 1)
                    if n == 0:
                        pe.wait_ge(v2_lo, g * NHALF + NHALF)
                    pe.wait_ge(c_o_lo, g * NB + n)
                    split_products(pe_, bank[5][:, :], v2h[:, n, :], v2l[:, n, :], pTh[:, n % 2, :], pTl[:, n % 2, :],
                                   True, True).then_inc(c_pv, 1)

                def merge(n):
                    pe.wait_ge(c_o_lo, g * NB + n + 1)
                    if n >= 2:
                        pe.wait_ge(c_acc, g * NB + n - 1)
                    for h in range(QH):
                        last = split_products(pe_, bank[6 + n % 2][:, :], o2h[:, n % 2, h, :], o2l[:, n % 2, h, :],
                                              xoh[:, h, :], xol[:, h, :], h == 0, h == QH - 1)
                    last.then_inc(c_wo, 1)

                for n in range(NB + 3):
                    if n < NB:
                        scores(n)
                    if 1 <= n <= NB:
                        turn(n - 1)
                    if 2 <= n <= NB + 1:
                        weigh(n - 2)
                    if n >= 3:
                        merge(n - 3)

            for b in range(NB):
                turn_stream(NB, b)

            pe.wait_ge(xt_lo, 2 * NB)
            with pe.Fori(0, NI) as i:
                for half in range(NHALF):
                    cols = slice(half * HALF, (half + 1) * HALF)
                    for m, done in ((0, f_gate), (1, f_up)):
                        if half == 0:
                            pe.wait_ge(f_wlo, i * 2 + m + 1)
                        pe.wait_ge(f_inter, i * NHALF + half)
                        project(bank[2 * half + m][:, :], [wgh[:, m, k * P:(k + 1) * P] for k in range(NK)],
                                [wgl[:, m, k * P:(k + 1) * P] for k in range(NK)], aTh, aTl, cols).then_inc(done, 1)

            pe.wait_ge(f_ilo, NI * NHALF)
            pe.wait_ge(f_dlo, NI)
            for b in range(NB):
                if b >= 2:
                    pe.wait_ge(f_y16, b - 1)
                for k in range(NI):
                    last = split_products(pe_, bank[4 + b % 2][:, :], inh[:, k, b * S:(b + 1) * S], inl[:, k, b * S:(b + 1) * S],
                                          wdh[:, k, :], wdl[:, k, :], k == 0, k == NI - 1)
                last.then_inc(f_y, 1)


def constants():
    ar = np.arange
    inv = (1.0 / np.float32(10000.0) ** (ar(0, DK, 2, dtype=np.float32) / np.float32(DK))).astype(np.float32)
    ang = (ar(S, dtype=np.float32)[None, :] * inv[:, None]).astype(np.float32)
    cos, sin = np.cos(ang).astype(np.float32), np.sin(ang).astype(np.float32)
    cos = np.concatenate([cos, cos], 0)
    sin = np.concatenate([sin, -sin], 0)
    root = np.float32(1.0 / np.sqrt(DK))
    part = ar(P)
    return {
        "ident": np.eye(P, dtype=np.float32),
        "tri": np.where(part[None, :] > part[:, None], np.float32(NEG), np.float32(0)).astype(np.float32),
        "hmask": (part[:, None] // HD1 == ar(HC)[None, :]).astype(np.float32),
        "cosq": cos * root, "sinq": sin * root, "cosk": cos, "sink": sin,
        "shq": (4 * (part % PACK)).astype(np.int32)[:, None],
        "shz": np.tile((4 * ar(PACK)).astype(np.int32)[None, :], (P, 1)),
    }


def layout(inputs):
    a = {k: np.asarray(v) for k, v in inputs.items()}
    r = {
        "x": a["x"], "xT": a["x"].reshape(T, D).T, "ctxT": a["ctx_4096"].reshape(T, D).T,
        "mask": a["mask_BxSxS2_ff1"],
        "wqT": a["L0_attn_Wq"].T, "wkT": a["L0_attn_Wk"].T, "wvT": a["L0_attn_Wv"].T, "woT": a["L0_attn_Wo"].T,
        "bq": a["L0_attn_bq"], "bk": a["L0_attn_bk"], "bv": a["L0_attn_bv"], "bo": a["L0_attn_bo"],
        "xwq": a["L0_xattn_wq"], "xwk": a["L0_xattn_wk"], "xwv": a["L0_xattn_wv"], "xwo": a["L0_xattn_wo"],
    }

    def rows(q):
        return np.repeat(q, PACK, axis=0)

    for s, name in (("g", "gate"), ("u", "up")):
        q, sc, z = (a[f"L0_ffn_{name}_{w}"] for w in ("qweight", "scales", "zeros"))
        q = np.pad(rows(q), ((0, 0), (0, IPAD - INTER)))
        sc = np.pad(sc, ((0, 0), (0, IPAD - INTER)))
        z = np.pad(z, ((0, 0), (0, (IPAD - INTER) // PACK)))
        r[s + "q"] = q.reshape(NK, P, NI, P).transpose(2, 1, 0, 3).reshape(NI, P, NK * P)
        r[s + "s"] = sc.reshape(NK, NI, P).transpose(1, 0, 2).reshape(NI, NK * P)
        r[s + "z"] = z.reshape(NK, NI, P // PACK).transpose(1, 0, 2).reshape(NI, NK * P // PACK)
    q = np.pad(rows(a["L0_ffn_down_qweight"]), ((0, IPAD - INTER), (0, 0)))
    r["dq"] = q.reshape(NI, P, D)
    r["ds"], r["dz"] = a["L0_ffn_down_scales"], a["L0_ffn_down_zeros"]
    return r


_ARGS = ["x", "xT", "ctxT", "mask", "wqT", "wkT", "wvT", "woT", "bq", "bk", "bv", "bo", "xwq", "xwk", "xwv", "xwo",
         "gq", "gs", "gz", "uq", "us", "uz", "dq", "ds", "dz",
         "ident", "tri", "hmask", "cosq", "sinq", "cosk", "sink", "shq", "shz"]


def kernel(**inputs):
    import concourse.bacc as bacc
    from concourse.bass_utils import run_bass_kernel_spmd

    nc = bacc.Bacc("TRN2", target_bir_lowering=False, num_devices=1)
    data = {**layout(inputs), **constants()}
    arrays, args = {}, []
    for name in _ARGS:
        arrays[f"in_{name}"] = np.ascontiguousarray(data[name])
        args.append(nc.dram_tensor(f"in_{name}", arrays[f"in_{name}"].shape,
                                   mybir.dt.from_np(arrays[f"in_{name}"].dtype), kind="ExternalInput").ap())
    out = nc.dram_tensor("out", (NB, S, D), F32, kind="ExternalOutput").ap()
    decoder_kernel(nc, *args, out)
    return run_bass_kernel_spmd(nc, [arrays], core_ids=[0]).results[0]["out"]
```
